# Optimizing a Trainium2 kernel written in Bass

```python
import numpy as np
import jax
import jax.numpy as jnp

def _softmax(x, axis=-1):
    return jax.nn.softmax(x, axis=axis)

def _gelu(x):
    return jax.nn.gelu(x, approximate=True)

def _silu(x):
    return jax.nn.silu(x)

def _sigmoid(x):
    return jax.nn.sigmoid(x)

def _layernorm(x, axis=-1, eps=1e-05):
    m = jnp.mean(x, axis=axis, keepdims=True)
    v = jnp.var(x, axis=axis, keepdims=True)
    return (x - m) / jnp.sqrt(v + eps)

def _scatter_add(tgt, idx, src, axis=0):
    return tgt.at[idx].add(src)

def _segment_sum(src, seg, n):
    return jax.ops.segment_sum(src, seg, n)
kernel_name = 'mk_xattn_seq_d2_seqx_r2_433d2f'

def setup_inputs(seed: int=0):
    np.random.seed(seed)
    _w = jnp.asarray

    def _rec_inputs():
        import jax
        import jax.numpy as jnp
        _rk = jax.random.key(seed)
        x = -0.0002928 + 1 * jax.random.normal(jax.random.fold_in(_rk, 1), (4, 1024, 512), jnp.float32)
        _lenS = 1024 - jax.random.randint(jax.random.fold_in(_rk, 7), (4,), 0, max(1, 1024 // 4) + 1, jnp.int32)
        _lenS2 = 1024 - jax.random.randint(jax.random.fold_in(_rk, 8), (4,), 0, max(1, 1024 // 4) + 1, jnp.int32)
        _ctx_1024P = jax.random.normal(jax.random.fold_in(_rk, 11), (4, 16, 512), jnp.float32)
        _ctx_1024c = jax.random.dirichlet(jax.random.fold_in(_rk, 511), 0.3 * jnp.ones((16,), jnp.float32), (4, 1024))
        _ctx_1024t = jnp.einsum('bsk,bkd->bsd', _ctx_1024c, _ctx_1024P)
        _ctx_1024t = _ctx_1024t * jax.lax.rsqrt(jnp.mean(jnp.square(_ctx_1024t)) + 1e-12) * 0.953939
        ctx_1024 = -1.39393e-06 + 0.999914 * (_ctx_1024t + 0.3 * jax.random.normal(jax.random.fold_in(_rk, 611), (4, 1024, 512), jnp.float32))
        return (x, ctx_1024)
    x, ctx_1024 = _rec_inputs()

    def _L0_xattn_setup():
        import jax, jax.numpy as jnp
        import numpy as np
        EPS = 1e-05

        def _layernorm(x, g, b):
            m = jnp.mean(x, axis=-1, keepdims=True)
            v = jnp.mean((x - m) ** 2, axis=-1, keepdims=True)
            return (x - m) / jnp.sqrt(v + EPS) * g + b

        def _mha(x, kv, Wq, Wk, Wv, mask, causal):
            m = mask[:, None]
            Q = jnp.einsum('bsd,hdk->bhsk', x, Wq) * m
            K = jnp.einsum('bsd,hdk->bhsk', kv, Wk) * m
            V = jnp.einsum('bsd,hdk->bhsk', kv, Wv) * m
            energy = jnp.einsum('bhsk,bhtk->bhst', Q, K)
            S = energy.shape[-1]
            lengths = jnp.sum(energy[:, :, 0, :] != 0, axis=-1)
            cols = jnp.arange(S)
            energy = jnp.where(cols[None, None, None, :] >= lengths[:, :, None, None], -jnp.inf, energy)
            if causal:
                energy = jnp.where(cols[None, :] > cols[:, None], -jnp.inf, energy)
            dk = Wq.shape[-1]
            score = jax.nn.softmax(energy / jnp.sqrt(jnp.asarray(dk, energy.dtype)), axis=-1)
            out = jnp.einsum('bhst,bhtk->bhsk', score, V) * m
            B, H, Sx, dkk = out.shape
            return out.transpose(0, 2, 1, 3).reshape(B, Sx, H * dkk)
        key = jax.random.key(seed)
        ks = jax.random.split(key, 20)
        B, S, D, H = (2, 1024, 512, 16)
        dk = D // H
        sd = 0.02
        inp = {'x': jax.random.normal(ks[0], (B, S, D), jnp.float32), 'context': jax.random.normal(ks[1], (B, S, D), jnp.float32), 'Wq1': jax.random.normal(ks[2], (H, D, dk), jnp.float32) * sd, 'Wk1': jax.random.normal(ks[3], (H, D, dk), jnp.float32) * sd, 'Wv1': jax.random.normal(ks[4], (H, D, dk), jnp.float32) * sd, 'Wq2': jax.random.normal(ks[5], (H, D, dk), jnp.float32) * sd, 'Wk2': jax.random.normal(ks[6], (H, D, dk), jnp.float32) * sd, 'Wv2': jax.random.normal(ks[7], (H, D, dk), jnp.float32) * sd, 'ln1_g': jnp.ones((D,), jnp.float32), 'ln1_b': jnp.zeros((D,), jnp.float32), 'ln2_g': jnp.ones((D,), jnp.float32), 'ln2_b': jnp.zeros((D,), jnp.float32), 'ln3_g': jnp.ones((D,), jnp.float32), 'ln3_b': jnp.zeros((D,), jnp.float32), 'fc1_w': jax.random.normal(ks[8], (D, D), jnp.float32) * sd, 'fc1_b': jnp.zeros((D,), jnp.float32), 'fc2_w': jax.random.normal(ks[9], (D, D), jnp.float32) * sd, 'fc2_b': jnp.zeros((D,), jnp.float32)}
        return inp
    _L0_xattn_all = _L0_xattn_setup()
    _L0_xattn_in = {k: v for k, v in _L0_xattn_all.items() if k in ('Wq1', 'Wk1', 'Wv1', 'Wq2', 'Wk2', 'Wv2', 'ln1_g', 'ln1_b', 'ln2_g', 'ln2_b', 'ln3_g', 'ln3_b', 'fc1_w', 'fc1_b', 'fc2_w', 'fc2_b')}
    del _L0_xattn_all

    def _L1_xattn_setup():
        import jax, jax.numpy as jnp
        import numpy as np
        B, SR, SF, D = (8, 1024, 1024, 512)
        key = jax.random.key(seed)
        k1, k2 = jax.random.split(key)
        H_real = jax.random.normal(k1, (B, SR, D), dtype=jnp.float32)
        H_fake = jax.random.normal(k2, (B, SF, D), dtype=jnp.float32)
        return {'H_real': H_real, 'H_fake': H_fake}
    _L1_xattn_all = _L1_xattn_setup()
    _L1_xattn_in = {k: v for k, v in _L1_xattn_all.items() if k in ()}
    del _L1_xattn_all
    return {'x': x, 'ctx_1024': ctx_1024, 'L0_xattn_Wq1': _L0_xattn_in['Wq1'], 'L0_xattn_Wk1': _L0_xattn_in['Wk1'], 'L0_xattn_Wv1': _L0_xattn_in['Wv1'], 'L0_xattn_Wq2': _L0_xattn_in['Wq2'], 'L0_xattn_Wk2': _L0_xattn_in['Wk2'], 'L0_xattn_Wv2': _L0_xattn_in['Wv2'], 'L0_xattn_ln1_g': _L0_xattn_in['ln1_g'], 'L0_xattn_ln1_b': _L0_xattn_in['ln1_b'], 'L0_xattn_ln2_g': _L0_xattn_in['ln2_g'], 'L0_xattn_ln2_b': _L0_xattn_in['ln2_b'], 'L0_xattn_ln3_g': _L0_xattn_in['ln3_g'], 'L0_xattn_ln3_b': _L0_xattn_in['ln3_b'], 'L0_xattn_fc1_w': _L0_xattn_in['fc1_w'], 'L0_xattn_fc1_b': _L0_xattn_in['fc1_b'], 'L0_xattn_fc2_w': _L0_xattn_in['fc2_w'], 'L0_xattn_fc2_b': _L0_xattn_in['fc2_b']}

def reference(x, ctx_1024, L0_xattn_Wq1, L0_xattn_Wk1, L0_xattn_Wv1, L0_xattn_Wq2, L0_xattn_Wk2, L0_xattn_Wv2, L0_xattn_ln1_g, L0_xattn_ln1_b, L0_xattn_ln2_g, L0_xattn_ln2_b, L0_xattn_ln3_g, L0_xattn_ln3_b, L0_xattn_fc1_w, L0_xattn_fc1_b, L0_xattn_fc2_w, L0_xattn_fc2_b):
    import jax
    import jax.numpy as jnp

    def _L0_xattn_ref(x, context, Wq1, Wk1, Wv1, Wq2, Wk2, Wv2, ln1_g, ln1_b, ln2_g, ln2_b, ln3_g, ln3_b, fc1_w, fc1_b, fc2_w, fc2_b):
        import jax, jax.numpy as jnp
        import numpy as np
        EPS = 1e-05

        def _layernorm(x, g, b):
            m = jnp.mean(x, axis=-1, keepdims=True)
            v = jnp.mean((x - m) ** 2, axis=-1, keepdims=True)
            return (x - m) / jnp.sqrt(v + EPS) * g + b

        def _mha(x, kv, Wq, Wk, Wv, mask, causal):
            m = mask[:, None]
            Q = jnp.einsum('bsd,hdk->bhsk', x, Wq) * m
            K = jnp.einsum('bsd,hdk->bhsk', kv, Wk) * m
            V = jnp.einsum('bsd,hdk->bhsk', kv, Wv) * m
            energy = jnp.einsum('bhsk,bhtk->bhst', Q, K)
            S = energy.shape[-1]
            lengths = jnp.sum(energy[:, :, 0, :] != 0, axis=-1)
            cols = jnp.arange(S)
            energy = jnp.where(cols[None, None, None, :] >= lengths[:, :, None, None], -jnp.inf, energy)
            if causal:
                energy = jnp.where(cols[None, :] > cols[:, None], -jnp.inf, energy)
            dk = Wq.shape[-1]
            score = jax.nn.softmax(energy / jnp.sqrt(jnp.asarray(dk, energy.dtype)), axis=-1)
            out = jnp.einsum('bhst,bhtk->bhsk', score, V) * m
            B, H, Sx, dkk = out.shape
            return out.transpose(0, 2, 1, 3).reshape(B, Sx, H * dkk)
        mask0 = 1.0 - jnp.all(x == 0, axis=2, keepdims=True).astype(x.dtype)
        z = _mha(x, x, Wq1, Wk1, Wv1, mask0, causal=True)
        x1 = _layernorm(x + z, ln1_g, ln1_b)
        mask1 = 1.0 - jnp.all(x1 == 0, axis=2, keepdims=True).astype(x1.dtype)
        z = _mha(x1, context, Wq2, Wk2, Wv2, mask1, causal=False)
        x2 = _layernorm(x1 + z, ln2_g, ln2_b)
        z = jnp.maximum(x2 @ fc1_w.T + fc1_b, 0.0) * mask0
        z = (z @ fc2_w.T + fc2_b) * mask0
        return _layernorm(x2 + z, ln3_g, ln3_b)

    def _L1_xattn_ref(H_real, H_fake):
        import jax, jax.numpy as jnp
        import numpy as np
        B, SR, SF, D = (8, 1024, 1024, 512)
        scores = jnp.einsum('brd,bfd->brf', H_real, H_fake)
        weights = jax.nn.softmax(scores, axis=-1)
        context = jnp.einsum('brf,bfd->brd', weights, H_fake)
        return H_real + context
    x = _L0_xattn_ref(x, ctx_1024, L0_xattn_Wq1, L0_xattn_Wk1, L0_xattn_Wv1, L0_xattn_Wq2, L0_xattn_Wk2, L0_xattn_Wv2, L0_xattn_ln1_g, L0_xattn_ln1_b, L0_xattn_ln2_g, L0_xattn_ln2_b, L0_xattn_ln3_g, L0_xattn_ln3_b, L0_xattn_fc1_w, L0_xattn_fc1_b, L0_xattn_fc2_w, L0_xattn_fc2_b)
    x = _L1_xattn_ref(x, ctx_1024)
    return x

_drawn_inputs = setup_inputs


def setup_inputs(seed=0):
    import zlib

    import numpy as np

    out = dict(_drawn_inputs(seed))
    spreads = {'L0_xattn_ln1_g': (1.0, 0.2),
     'L0_xattn_ln1_b': (0.0, 0.1),
     'L0_xattn_ln2_g': (1.0, 0.2),
     'L0_xattn_ln2_b': (0.0, 0.1),
     'L0_xattn_ln3_g': (1.0, 0.2),
     'L0_xattn_ln3_b': (0.0, 0.1),
     'L0_xattn_fc1_b': (0.0, 0.1),
     'L0_xattn_fc2_b': (0.0, 0.1)}
    factors = {'L0_xattn_Wq1': 2.878}
    for name, (base, spread) in spreads.items():
        noise = np.random.default_rng([zlib.crc32(name.encode()), seed]).standard_normal(out[name].shape)
        drawn = base * np.exp(spread * noise) if base else spread * noise
        out[name] = jnp.asarray(drawn.astype(out[name].dtype))
    for name, factor in factors.items():
        out[name] = (out[name] * factor).astype(out[name].dtype)
    return out
```

```python
from contextlib import ExitStack

import numpy as np

import concourse.bass as bass
from concourse import mybir

F32 = mybir.dt.float32
F32R = mybir.dt.float32r
ALU = mybir.AluOpType
ACT = mybir.ActivationFunctionType
AX = mybir.AxisListType

P = 128
B, S, D, H = 4, 1024, 512, 16
DK = D // H
NC = S // P
ND = D // P
HALF = 512
NS = S // HALF
HPG = P // DK
NG = H // HPG
GROUPS = B * NG
EPS = 1e-5
NEG = -1e30
SCALE = float(DK) ** -0.5

K_MAX = 3 * DK + 1
M_ROWS = 1 + 2 * NC
K_EXP = 3 * DK + M_ROWS
TERMS = ((0, 0), (1, 0), (0, 1))


def wait(eng, sem, value):
    if isinstance(value, int) and value <= 0:
        return
    eng.wait_ge(sem, value)


def wait_apart(eng, sem, value, passed):
    if isinstance(value, int):
        return wait(eng, sem, value)
    eng.wait_ge(sem, value)
    eng.sem_inc(passed, 1)


def f32(ap):
    return ap.bitcast(F32)


class Space:

    def __init__(self, nc, ctx, stage):
        self.nc, self.ctx, self.stage, self.sems = nc, ctx, stage, []

    def sb(self, name, shape, dt=F32):
        return self.ctx.enter_context(self.nc.sbuf_tensor(f"{self.stage}_{name}", shape, dt))

    def bank(self, name):
        return self.ctx.enter_context(self.nc.psum_tensor(f"{self.stage}_{name}", [P, HALF], F32))

    def sem(self, name):
        self.sems.append(self.ctx.enter_context(self.nc.semaphore(f"{self.stage}_{name}")))
        return self.sems[-1]

    def block(self):
        self.ctx.callback(self.clear)
        return self.ctx.enter_context(self.nc.Block())

    def clear(self):
        with self.nc.Block() as block:
            @block.sync
            def _(sp):
                for sem in self.sems:
                    sp.sem_clear(sem)


def project(nc, stage, q_src, kv_src, key_mask, wq, wk, wv, sel, iota, scr):
    q_split, k_split, v_heads, len_mask = scr
    with ExitStack() as ctx:
        s = Space(nc, ctx, stage)
        w_hi = [s.sb(f"w_hi{i}", [P, ND, D], F32R) for i in range(3)]
        w_lo = [s.sb(f"w_lo{i}", [P, ND, D], F32R) for i in range(3)]
        w_raw = s.sb("w_raw", [P, ND, D])
        raw = [s.sb(f"raw{h}", [P, ND, HALF]) for h in range(NS)]
        src = [[s.sb(f"src{k}{t}", [P, ND, S], F32R) for t in ("hi", "lo")] for k in range(2)]
        st = [[s.sb(f"stage{i}{t}", [P, S], F32R) for t in ("hi", "lo")] for i in range(2)]
        vb = s.sb("v_batch", [P, H, NC * DK])
        keep = s.sb("keep", [P, S]) if key_mask is not None else None
        q0 = [s.sb(f"q0{t}", [P, ND, P], F32R) for t in ("hi", "lo")]
        sel_sb = s.sb("sel", [P, ND, H])
        iota_sb = s.sb("iota", [H, S])
        nonzero = s.sb("nonzero", [H, NS, HALF])
        count = s.sb("count", [H, NS])
        length = s.sb("length", [H, 1])
        mrow = s.sb("mrow", [H, S], F32R)
        pj = [s.bank(f"pj{i}") for i in range(4)]
        e0 = [s.bank(f"e0{i}") for i in range(NS)]

        consts_in = s.sem("consts_in")
        w_in = s.sem("w_in")
        w_split_hi = s.sem("w_split_hi")
        w_split = s.sem("w_split")
        raw_in = [s.sem(f"raw_in{h}") for h in range(NS)]
        keep_in = s.sem("keep_in")
        masked = s.sem("masked")
        split_hi = s.sem("split_hi")
        split = s.sem("split")
        pj_done = s.sem("pj_done")
        hi_done = s.sem("hi_done")
        lo_done = s.sem("lo_done")
        q0_zero = s.sem("q0_zero")
        q0_done = s.sem("q0_done")
        e0_done = s.sem("e0_done")
        counted = s.sem("counted")
        length_done = s.sem("length_done")
        mrow_done = s.sem("mrow_done")
        v_done = s.sem("v_done")
        staged_out = [s.sem(f"staged_out{i}") for i in range(2)]
        v_out = s.sem("v_out")
        mrow_out = s.sem("mrow_out")

        weights = (wq, wk, wv)
        BLOCKS = 8 + 8 + NC

        block = s.block()

        @block.sync
        def _(sp):
            def load_w(i):
                wait(sp, w_split, i)
                sp.dma_start(w_raw[:, :, :], weights[i].rearrange("(t p) n -> p t n", p=P)).then_inc(w_in, 16)

            def load_source(b, kv):
                k = 2 * b + kv
                if kv and key_mask is not None:
                    wait(sp, split, 4 * b)
                    sp.dma_start(keep[:, :], key_mask[b, :].partition_broadcast(P)).then_inc(keep_in, 16)
                source = kv_src if kv else q_src
                for h in range(NS):
                    wait(sp, split, 2 * (k - 1) + h + 1)
                    sp.dma_start(raw[h][:, :, :], source[b, :, h * HALF:(h + 1) * HALF]
                                 .rearrange("(t p) s -> p t s", p=P)).then_inc(raw_in[h], 16)

            def store_stage(b, which, dst, groups=range(NG)):
                for g in groups:
                    i = g % 2
                    sp.wait_ge(lo_done, 16 * b + 8 * which + 2 * g + 2)
                    for part in range(2):
                        rows = dst[part, :, :].rearrange("(r p) s -> r p s", p=P)
                        sp.dma_start(rows[b * NG + g, :, :], f32(st[i][part][:, :])).then_inc(staged_out[i], 16)

            def batch(b, last):
                store_stage(b, 0, q_split, range(2))
                if not last:
                    load_source(b + 1, 0)
                store_stage(b, 0, q_split, range(2, NG))
                store_stage(b, 1, k_split)
                if not last:
                    load_source(b + 1, 1)
                sp.wait_ge(v_done, NC * (b + 1))
                sp.dma_start(v_heads.rearrange("(b h) p f -> b p h f", h=H)[b, :, :, :], vb[:, :, :]).then_inc(v_out, 16)
                sp.wait_ge(mrow_done, b + 1)
                sp.dma_start(len_mask.rearrange("(b h) t -> b h t", h=H)[b, :, :], f32(mrow[:, :])).then_inc(mrow_out, 16)

            load_w(0)
            load_source(0, 0)
            sp.dma_start(sel_sb[:, :, :], sel).then_inc(consts_in, 16)
            sp.dma_start(iota_sb[:, :], iota).then_inc(consts_in, 16)
            load_w(1)
            load_source(0, 1)
            load_w(2)
            batch(0, False)
            with sp.Fori(1, B - 1) as b:
                batch(b, False)
            batch(B - 1, True)
            for i in range(2):
                sp.wait_ge(staged_out[i], 32 * NG * B)
            sp.wait_ge(v_out, 16 * B)
            sp.wait_ge(mrow_out, 16 * B)

        @block.tensor
        def _(pe):
            def bank_free(b, k):
                if k < 4:
                    wait(pe, v_done, NC * b + k - 3)
                elif k < 20:
                    wait(pe, lo_done, 16 * b + k - 3)
                else:
                    wait(pe, v_done, NC * b + k - 19)

            def features(b, which):
                if isinstance(b, int) and b == 0:
                    pe.wait_ge(w_split, which + 1)
                for g in range(NG):
                    for h in range(NS):
                        k = 8 * which + 2 * g + h
                        pe.wait_ge(split, 4 * b + 2 * which + h + 1)
                        bank_free(b, k)
                        for n, (wt, xt) in enumerate(TERMS):
                            for d in range(ND):
                                w = (w_hi, w_lo)[wt][which]
                                last = pe.matmul(pj[k % 4][:, :], w[:, d, g * P:(g + 1) * P],
                                                 src[which][xt][:, d, h * HALF:(h + 1) * HALF],
                                                 start=(n == 0 and d == 0), stop=(n == 2 and d == ND - 1))
                        last.then_inc(pj_done, 1)
                    if which and g:
                        energies0(b, g - 1)

            def energies0(b, g):
                if g == 0:
                    pe.wait_ge(q0_done, 2 * NG * (b + 1))
                    wait(pe, counted, NS * b)
                pe.wait_ge(lo_done, 16 * b + 8 + 2 * g + 2)
                for h in range(NS):
                    for n, (qt, kt) in enumerate(TERMS):
                        last = pe.matmul(e0[h][:, :], q0[qt][:, g, :], st[g % 2][kt][:, h * HALF:(h + 1) * HALF],
                                         start=(g == 0 and n == 0), stop=(g == NG - 1 and n == 2))
                last.then_inc(e0_done, 1)

            def batch(b):
                features(b, 0)
                features(b, 1)
                if isinstance(b, int) and b == 0:
                    pe.wait_ge(w_split, 3)
                for c in range(NC):
                    k = 16 + c
                    bank_free(b, k)
                    for n, (xt, wt) in enumerate(TERMS):
                        for d in range(ND):
                            last = pe.matmul(pj[k % 4][:, :], src[1][xt][:, d, c * P:(c + 1) * P],
                                             (w_hi, w_lo)[wt][2][:, d, :],
                                             start=(n == 0 and d == 0), stop=(n == 2 and d == ND - 1))
                    last.then_inc(pj_done, 1)
                    if c == 0:
                        energies0(b, NG - 1)

            batch(0)
            with pe.Fori(1, B) as b:
                batch(b)

        @block.scalar
        def _(act):
            def first_halves(b, which):
                for g in range(NG):
                    for h in range(NS):
                        k = 8 * which + 2 * g + h
                        if h == 0:
                            wait(act, staged_out[g % 2], 32 * (NG * b + 2 * which + g // 2))
                            if which and g >= 2:
                                act.wait_ge(e0_done, NG * b + g - 1)
                            elif which:
                                act.wait_ge(q0_done, 2 * (NG * b + g + 3))
                            elif g >= 2:
                                act.wait_ge(q0_done, 2 * (NG * b + g - 1))
                            else:
                                wait(act, e0_done, NG * b + g - 1)
                        act.wait_ge(pj_done, BLOCKS * b + k + 1)
                        act.activation(st[g % 2][0][:, h * HALF:(h + 1) * HALF], pj[k % 4][:, :], ACT.Copy)\
                           .then_inc(hi_done, 1)

            def batch(b):
                first_halves(b, 0)
                first_halves(b, 1)
                for c in range(NC):
                    if c == 0:
                        wait(act, v_out, 16 * b)
                    act.wait_ge(pj_done, BLOCKS * b + 17 + c)
                    act.activation(vb[:, :, c * DK:(c + 1) * DK],
                                   pj[c % 4][:, :].rearrange("p (h k) -> p h k", h=H), ACT.Copy).then_inc(v_done, 1)

            batch(0)
            with act.Fori(1, B) as b:
                batch(b)

        @block.vector
        def _(dve):
            def split_w(i):
                dve.wait_ge(w_in, 16 * (i + 1))
                dve.tensor_copy(w_hi[i][:, :, :], w_raw[:, :, :]).then_inc(w_split_hi, 1)
                dve.wait_ge(w_split_hi, i + 1)
                dve.tensor_tensor(w_lo[i][:, :, :], w_raw[:, :, :], f32(w_hi[i][:, :, :]), ALU.subtract)\
                   .then_inc(w_split, 1)

            def split_source(b, kv):
                k = 2 * b + kv
                wait(dve, pj_done, BLOCKS * b if kv else BLOCKS * (b - 1) + 8)
                for h in range(NS):
                    cols = slice(h * HALF, (h + 1) * HALF)
                    dve.wait_ge(raw_in[h], 16 * (k + 1))
                    if kv and key_mask is not None:
                        if h == 0:
                            dve.wait_ge(keep_in, 16 * (b + 1))
                        for d in range(ND):
                            dve.tensor_tensor(raw[h][:, d, :], raw[h][:, d, :], keep[:, cols], ALU.mult)\
                               .then_inc(masked, 1)
                        dve.wait_ge(masked, ND * (NS * b + h + 1))
                    dve.tensor_copy(src[kv][0][:, :, cols], raw[h][:, :, :]).then_inc(split_hi, 1)
                    dve.wait_ge(split_hi, 2 * k + h + 1)
                    dve.tensor_tensor(src[kv][1][:, :, cols], raw[h][:, :, :], f32(src[kv][0][:, :, cols]),
                                      ALU.subtract).then_inc(split, 1)

            def second_halves(b, which, between=None):
                for g in range(NG):
                    if between and g:
                        between[g - 1]()
                    for h in range(NS):
                        k = 8 * which + 2 * g + h
                        cols = slice(h * HALF, (h + 1) * HALF)
                        dve.wait_ge(hi_done, 16 * b + k + 1)
                        dve.tensor_tensor(st[g % 2][1][:, cols], pj[k % 4][:, :], f32(st[g % 2][0][:, cols]),
                                          ALU.subtract).then_inc(lo_done, 1)
                        if h == 0 and not which:
                            if g == 0:
                                wait(dve, e0_done, NG * b)
                            dve.wait_ge(lo_done, 16 * b + k + 1)
                            for part in range(2):
                                dve.tensor_scalar(q0[part][:, g, 0:H], sel_sb[:, g, :], f32(st[g % 2][part][:, 0:1]),
                                                  None, ALU.mult).then_inc(q0_done, 1)

            def key_masks(b):
                dve.wait_ge(e0_done, NG * (b + 1))
                wait(dve, length_done, b)
                for h in range(NS):
                    dve.tensor_scalar(nonzero[:, h, :], e0[h][0:H, :], 0.0, None, ALU.not_equal)\
                       .then_inc(counted, 1)
                dve.wait_ge(counted, NS * (b + 1))
                dve.tensor_reduce(length[:, :], nonzero[:, :, :], AX.XY, ALU.add).then_inc(length_done, 1)
                dve.wait_ge(length_done, b + 1)
                wait(dve, mrow_out, 16 * b)
                dve.tensor_scalar(mrow[:, :], iota_sb[:, :], length[:, 0:1], NEG, ALU.is_ge, ALU.mult)\
                   .then_inc(mrow_done, 1)

            def batch(b, last):
                first = isinstance(b, int) and b == 0
                second_halves(b, 0, (lambda: split_w(1), lambda: split_source(0, 1), lambda: split_w(2)) if first else None)
                if not last:
                    split_source(b + 1, 0)
                second_halves(b, 1)
                key_masks(b)
                if not last:
                    split_source(b + 1, 1)

            for part in range(2):
                dve.memset(f32(q0[part][:, :, :]), 0.0).then_inc(q0_zero, 1)
            split_w(0)
            split_source(0, 0)
            dve.wait_ge(q0_zero, 2)
            dve.wait_ge(consts_in, 32)
            batch(0, False)
            with dve.Fori(1, B - 1) as b:
                batch(b, False)
            batch(B - 1, True)


def attend(nc, stage, causal, ident, blk17, tri, scr, z_groups):
    q_split, k_split, v_heads, len_mask = scr

    def key_tile_blocks(i):
        return [(h, max(h * HALF, i * P if causal else 0), (h + 1) * HALF)
                for h in range(NS) if not causal or i * P < (h + 1) * HALF]

    def query_tile_blocks(j):
        end = (j + 1) * P if causal else S
        return [(h, h * HALF, min((h + 1) * HALF, end)) for h in range(NS) if h * HALF < end]

    NE = sum(len(key_tile_blocks(i)) for i in range(NC))
    NM = sum(len(query_tile_blocks(j)) for j in range(NC))
    e_before = [sum(len(key_tile_blocks(i)) for i in range(t)) for t in range(NC + 1)]
    m_before = [sum(len(query_tile_blocks(j)) for j in range(t)) for t in range(NC + 1)]
    MAX_STEPS = [(1, i + NC // 2) if i < NC // 2 else (2, i - NC // 2) for i in range(NC)]
    LAG = 2 if causal else 3
    NEGATE_STEP, TURN_STEP = NC // 2 - 1, 5 if causal else 6
    COPY_STEP, TURN_ACC_STEP, OUT_STEP = LAG - 1, 3, 4
    RING = 4
    E_BANKS, M_BANKS = (3, 3) if causal else (4, 2)
    assert NE % E_BANKS == 0 and NM % M_BANKS == 0 and HPG == RING

    with ExitStack() as ctx:
        s = Space(nc, ctx, stage)
        qst = [s.sb(f"q_stack{i}", [P, S], F32R) for i in range(RING)]
        kst = [s.sb(f"k_stack{i}", [P, S], F32R) for i in range(RING)]
        vst = [s.sb(f"v{i}", [P, NC * DK]) for i in range(RING)]
        pt = [s.sb(f"weights{i}", [P, S]) for i in range(RING)]
        ones = s.sb("ones", [P, DK])
        mparts = [s.sb(f"max_parts{i}", [P, NC, NS]) for i in range(2)]
        negmax = s.sb("negmax", [P, NC])
        m17 = s.sb("m17", [P, M_ROWS], F32R)
        pair = None if causal else [s.sb(f"pair{i}", [P, S]) for i in range(2)]
        acc_sb = s.sb("acc_sb", [P, HALF])
        rden = s.sb("rden", [P, HPG, NS] if causal else [P, NS, HPG])
        zg = s.sb("z_group", [P, NC, P])
        blk = s.sb("blk", [P, NC, P])
        tri_sb = s.sb("tri", [P, HALF]) if causal else None
        mx = [s.bank(f"mx{i}") for i in range(M_BANKS)]
        et = [s.bank(f"et{i}") for i in range(E_BANKS)]
        acc = s.bank("acc")
        trb = s.bank("turned")

        consts_in = s.sem("consts_in")
        ready = s.sem("ready")
        qk_in = [s.sem(f"qk_in{i}") for i in range(RING)]
        v_in = [s.sem(f"v_in{i}") for i in range(RING)]
        mx_done = s.sem("mx_done")
        red_done = s.sem("red_done")
        nm_done = s.sem("nm_done")
        nm_hi_done = s.sem("nm_hi_done")
        m17_done = s.sem("m17_done")
        m17_turned = s.sem("m17_turned")
        qrow_done = s.sem("qrow_done")
        et_done = s.sem("et_done")
        exp_done = s.sem("exp_done")
        cut_done = s.sem("cut_done")
        pair_done = s.sem("pair_done")
        av_done = s.sem("av_done")
        acc_copied = s.sem("acc_copied")
        acc_turned = s.sem("acc_turned")
        rden_done = s.sem("rden_done")
        z_done = s.sem("z_done")
        z_out = s.sem("z_out")
        passed = s.sem("passed")

        def groups(eng, run):
            run(0)
            with eng.Fori(1, GROUPS - 1) as it:
                run(it)
            run(GROUPS - 1)

        def has(it, u, ahead):
            return not (isinstance(it, int) and it == GROUPS - 1 and u + ahead >= HPG)

        def before(it, u):
            if u:
                return it, u - 1
            return None if isinstance(it, int) and it == 0 else (it - 1, HPG - 1)

        block = s.block()

        @block.sync
        def _(sp):
            q_rows = [q_split[part, :, :].rearrange("(n k) s -> n k s", k=DK) for part in range(2)]
            k_rows = [k_split[part, :, :].rearrange("(n k) s -> n k s", k=DK) for part in range(2)]

            def load(it, u):
                n = HPG * it + u
                wait(sp, et_done, NE * (n - 3))
                wait(sp, qrow_done, n - 3)
                for r, part in enumerate((0, 0, 1)):
                    sp.dma_start(f32(kst[u][r * DK:(r + 1) * DK, :]), k_rows[part][n, :, :]).then_inc(qk_in[u], 16)
                for r, part in enumerate((0, 1, 0)):
                    sp.dma_start(f32(qst[u][r * DK:(r + 1) * DK, :]), q_rows[part][n, :, :]).then_inc(qk_in[u], 16)
                sp.dma_start(f32(kst[u][3 * DK:K_MAX, :]), len_mask[n, :].unsqueeze(0)).then_inc(qk_in[u], 16)
                wait(sp, av_done, NC * (n - 3))
                sp.dma_start(vst[u][:, :], v_heads[n, :, :]).then_inc(v_in[u], 16)

            def store(it):
                sp.wait_ge(z_done, HPG * (it + 1))
                sp.dma_start(z_groups[it, :, :].rearrange("(c p) f -> p c f", p=P), zg[:, :, :]).then_inc(z_out, 16)

            def group(it):
                for u in range(HPG):
                    if has(it, u, 2):
                        load(it + (u + 2) // HPG, (u + 2) % HPG)
                    if u == 0 and not (isinstance(it, int) and it == 0):
                        store(it - 1)

            sp.dma_start(blk[3 * DK:K_EXP, :, :], blk17).then_inc(consts_in, 16)
            if causal:
                sp.dma_start(tri_sb[:, :], tri).then_inc(consts_in, 16)
            sp.wait_ge(ready, 2 * RING)
            load(0, 0)
            load(0, 1)
            groups(sp, group)
            store(GROUPS - 1)
            sp.wait_ge(z_out, 16 * GROUPS)

        @block.tensor
        def _(pe):
            def max_tile(it, u, j):
                n = HPG * it + u
                if j == 0:
                    pe.wait_ge(qk_in[u], 7 * 16 * (it + 1))
                for x, (h, a, z) in enumerate(query_tile_blocks(j)):
                    k = m_before[j] + x
                    wait(pe, red_done, NM * n + k - M_BANKS + 1)
                    pe.matmul(mx[k % M_BANKS][:, 0:z - a], qst[u][0:K_MAX, j * P:(j + 1) * P], kst[u][0:K_MAX, a:z],
                              start=True, stop=True).then_inc(mx_done, 1)

            def turn_max(n):
                pe.wait_ge(m17_done, n + 1)
                wait(pe, z_done, n - 1)
                pe.transpose(trb[0:M_ROWS, 0:P], f32(m17[:, :]), ident[:, :]).then_inc(m17_turned, 1)

            def exp_tile(it, u, i):
                n = HPG * it + u
                if i == 0:
                    pe.wait_ge(qrow_done, n + 1)
                for x, (h, a, z) in enumerate(key_tile_blocks(i)):
                    k = e_before[i] + x
                    wait(pe, exp_done, NE * n + k - E_BANKS + 1)
                    pe.matmul(et[k % E_BANKS][:, 0:z - a], kst[u][0:K_EXP, i * P:(i + 1) * P], qst[u][0:K_EXP, a:z],
                              start=True, stop=True).then_inc(et_done, 1)

            def values_tile(it, u, i):
                n = HPG * it + u
                if i == 0:
                    pe.wait_ge(v_in[u], 16 * (it + 1))
                    wait(pe, acc_copied, n)
                pe.wait_ge(exp_done, NE * n + e_before[i + 1])
                if causal:
                    pe.wait_ge(cut_done, NC * n + i + 1)
                if causal:
                    for h, a, z in key_tile_blocks(i):
                        last_tile = (h + 1) * (NC // NS) - 1
                        for row, lhs in ((h * DK, vst[u][:, i * DK:(i + 1) * DK]), ((NS + h) * DK, ones[:, :])):
                            last = pe.matmul(acc[row:row + DK, a - h * HALF:z - h * HALF], lhs, pt[i % RING][:, a:z],
                                             start=(i == 0), stop=(i == last_tile), tile_position=(0, row))
                else:
                    last = quarters(0, vst[u][:, i * DK:(i + 1) * DK], pt[i % RING], i == 0)
                    if i % 2:
                        pe.wait_ge(pair_done, NC // 2 * n + i // 2 + 1)
                        last = quarters(2 * P, ones[:, :], pair[i // 2 % 2], False)
                last.then_inc(av_done, 1)

            def quarters(at, lhs, weights, start):
                by_quarter = weights[:, :].rearrange("p (a r s) -> p r a s", a=2, s=P)
                for r in range(HPG):
                    dst = acc[r * DK:(r + 1) * DK, at:at + 2 * P].rearrange("p (a s) -> p a s", s=P)
                    last = pe.matmul(dst, lhs, by_quarter[:, r, :, :], start=start, stop=False,
                                     tile_position=(0, r * DK), skip_group_check=True)
                return last

            def turn_acc(n):
                pe.wait_ge(acc_copied, n + 1)
                wait(pe, z_done, n)
                for j in range(HPG):
                    last = pe.transpose(trb[:, j * P:(j + 1) * P], acc_sb[:, j * P:(j + 1) * P], ident[:, :])
                last.then_inc(acc_turned, 1)

            def group(it):
                for u in range(HPG):
                    n = HPG * it + u
                    for i in range(NC):
                        exp_tile(it, u, i)
                        ahead, j = MAX_STEPS[i]
                        if has(it, u, ahead):
                            max_tile(it + (u + ahead) // HPG, (u + ahead) % HPG, j)
                        if i == TURN_STEP and has(it, u, 1):
                            turn_max(n + 1)
                        if i >= LAG:
                            values_tile(it, u, i - LAG)
                        elif before(it, u):
                            values_tile(*before(it, u), NC + i - LAG)
                        if i == TURN_ACC_STEP and before(it, u):
                            turn_acc(n - 1)

            pe.wait_ge(ready, 2 * RING + 4)
            for j in range(NC):
                max_tile(0, 0, j)
            turn_max(0)
            for j in range(NC // 2):
                max_tile(0, 1, j)
            groups(pe, group)
            for i in range(NC - LAG, NC):
                values_tile(GROUPS - 1, HPG - 1, i)
            turn_acc(HPG * GROUPS - 1)

        @block.scalar
        def _(act):
            def copy_acc(n):
                act.wait_ge(av_done, NC * (n + 1))
                wait(act, acc_turned, n)
                act.activation(acc_sb[:, :], acc[:, :], ACT.Copy).then_inc(acc_copied, 1)

            def group(it):
                for u in range(HPG):
                    n = HPG * it + u
                    for i in range(NC):
                        wait(act, av_done, NC * n + i - RING + 1)
                        if not causal:
                            wait(act, pair_done, NC // 2 * n + i // 2 - 1)
                        for x, (h, a, z) in enumerate(key_tile_blocks(i)):
                            k = e_before[i] + x
                            act.wait_ge(et_done, NE * n + k + 1)
                            act.activation(pt[i % RING][:, a:z], et[k % E_BANKS][:, 0:z - a], ACT.Exp, scale=SCALE)\
                               .then_inc(exp_done, 1)
                        if i == COPY_STEP and before(it, u):
                            copy_acc(n - 1)

            groups(act, group)
            copy_acc(HPG * GROUPS - 1)

        if causal:
            @block.gpsimd
            def _(pool):
                def group(it):
                    for u in range(HPG):
                        for i in range(NC):
                            n = HPG * it + u
                            wait_apart(pool, exp_done, NE * n + e_before[i] + 1, passed)
                            part = pt[i % RING][:, i * P:(i + 1) * P]
                            pool.affine_select(out=part, in_=part, pattern=[[1, P]], compare_op=ALU.is_ge,
                                               fill=0.0, base=0, channel_multiplier=-1).then_inc(cut_done, 1)

                groups(pool, group)

        else:
            @block.gpsimd
            def _(pool):
                def group(it):
                    for u in range(HPG):
                        n = HPG * it + u
                        for i in range(1, NC, 2):
                            pool.wait_ge(exp_done, NE * n + e_before[i + 1])
                            wait(pool, av_done, NC * n + i - 3)
                            pool.tensor_tensor(pair[i // 2 % 2][:, :], pt[(i - 1) % RING][:, :], pt[i % RING][:, :], ALU.add)\
                                .then_inc(pair_done, 1)

                groups(pool, group)

        @block.vector
        def _(dve):
            def reduce_blocks(it, u, j):
                n = HPG * it + u
                blocks = query_tile_blocks(j)
                for x, (h, a, z) in enumerate(blocks):
                    k = m_before[j] + x
                    cut = causal and x == len(blocks) - 1
                    if cut:
                        wait_apart(dve, mx_done, NM * n + k + 1, passed)
                    else:
                        dve.wait_ge(mx_done, NM * n + k + 1)
                    out = mparts[u % 2][:, j, h:h + 1]
                    scores = mx[k % M_BANKS][:, 0:z - a]
                    if cut:
                        dve.tensor_tensor_reduce(out=scores, in0=scores, in1=tri_sb[:, HALF - (z - a):HALF],
                                                 scale=1.0, scalar=-3e38, op0=ALU.add, op1=ALU.max,
                                                 accum_out=out).then_inc(red_done, 1)
                    else:
                        dve.tensor_reduce(out, scores, AX.X, ALU.max).then_inc(red_done, 1)

            def negate_max(it, u):
                n = HPG * it + u
                dve.wait_ge(red_done, NM * (n + 1))
                dve.tensor_reduce(negmax[:, :], mparts[u % 2][:, :, :], AX.X, ALU.max, negate=True)\
                   .then_inc(nm_done, 1)
                dve.wait_ge(nm_done, n + 1)
                wait(dve, m17_turned, n)
                dve.tensor_copy(m17[:, 1:1 + NC], negmax[:, :]).then_inc(nm_hi_done, 1)
                dve.wait_ge(nm_hi_done, n + 1)
                dve.tensor_tensor(m17[:, 1 + NC:M_ROWS], negmax[:, :], f32(m17[:, 1:1 + NC]), ALU.subtract)\
                   .then_inc(m17_done, 1)

            def max_rows(it, u):
                n = HPG * it + u
                dve.wait_ge(m17_turned, n + 1)
                dve.tensor_tensor(qst[u][3 * DK:K_EXP, :].rearrange("r (c f) -> r c f", c=NC),
                                  trb[0:M_ROWS, 0:P].unsqueeze(1).broadcast_to([M_ROWS, NC, P]),
                                  blk[3 * DK:K_EXP, :, :], ALU.mult).then_inc(qrow_done, 1)

            def outputs(it, u):
                n = HPG * it + u
                dve.wait_ge(acc_turned, n + 1)
                wait(dve, z_done, n)
                turned = trb[:, :].rearrange("p (j f) -> p j f", j=HPG)
                if causal:
                    z_tiles = zg[:, :, u * DK:(u + 1) * DK].rearrange("p (h j) k -> p j h k", h=NS)
                    values, sums = turned[:, :, 0:NS * DK].rearrange("p j (h k) -> p j h k", h=NS), turned[:, :, NS * DK:P:DK]
                else:
                    z_tiles = zg[:, :, u * DK:(u + 1) * DK].rearrange("p (a r) k -> p a r k", a=2)
                    values, sums = turned[:, 0:2, :].rearrange("p a (r k) -> p a r k", r=HPG), turned[:, 2:4, 0:P:DK]
                dve.reciprocal(rden[:, :, :], sums).then_inc(rden_done, 1)
                dve.wait_ge(rden_done, n + 1)
                if u == 0:
                    wait(dve, z_out, 16 * it)
                dve.tensor_tensor(z_tiles, values, rden[:, :, :].unsqueeze(3).broadcast_to(list(values.shape)), ALU.mult)\
                   .then_inc(z_done, 1)

            def group(it):
                for u in range(HPG):
                    nxt = (it + (u + 1) // HPG, (u + 1) % HPG)
                    for i in range(NC):
                        ahead, j = MAX_STEPS[i]
                        if has(it, u, ahead):
                            reduce_blocks(it + (u + ahead) // HPG, (u + ahead) % HPG, j)
                        if i == NEGATE_STEP and has(it, u, 1):
                            negate_max(*nxt)
                        if i == OUT_STEP and before(it, u):
                            outputs(*before(it, u))
                        if i == TURN_STEP and has(it, u, 1):
                            max_rows(*nxt)

            for i in range(RING):
                dve.memset(f32(qst[i][3 * DK:P, :]), 1.0).then_inc(ready, 1)
                dve.memset(f32(kst[i][3 * DK:P, :]), 1.0).then_inc(ready, 1)
            for i in range(2):
                dve.memset(mparts[i][:, :, :], -3e38).then_inc(ready, 1)
            dve.memset(ones[:, :], 1.0).then_inc(ready, 1)
            dve.memset(f32(m17[:, 0:1]), 1.0).then_inc(ready, 1)
            dve.wait_ge(ready, 2 * RING + 4)
            dve.wait_ge(consts_in, 32 if causal else 16)
            for j in range(NC):
                reduce_blocks(0, 0, j)
            negate_max(0, 0)
            max_rows(0, 0)
            for j in range(NC // 2):
                reduce_blocks(0, 1, j)
            groups(dve, group)
            outputs(GROUPS - 1, HPG - 1)


def batches(eng, run):
    run(0)
    with eng.Fori(1, B - 1) as b:
        run(b)
    run(B - 1)


def tile_before(b, c, back):
    if c >= back:
        return b, c - back
    return None if isinstance(b, int) and b == 0 else (b - 1, c - back + NC)


def tile_after(b, c, ahead):
    if c + ahead < NC:
        return b, c + ahead
    return None if isinstance(b, int) and b == B - 1 else (b + 1, c + ahead - NC)


def norm1(nc, stage, ident, x_rows, z_groups, g_row, b_row, keep0, keep1, x1_rows, x1t, key_mask):
    with ExitStack() as ctx:
        s = Space(nc, ctx, stage)
        R = 4
        AHEAD = 6
        g_sb, b_sb = s.sb("gain", [P, D]), s.sb("shift", [P, D])
        x = [s.sb(f"x{i}", [P, D]) for i in range(NC)]
        z = [s.sb(f"z{i}", [P, HPG, P]) for i in range(NC)]
        y = [s.sb(f"y{i}", [P, D]) for i in range(R)]
        xn = [s.sb(f"xn{i}", [P, D]) for i in range(R)]
        x1 = [s.sb(f"x1{i}", [P, D]) for i in range(R)]
        x1t_sb = [s.sb(f"x1t{i}", [P, ND, P]) for i in range(R)]
        abs_out = [[s.sb(f"abs{k}{i}", [P, D]) for i in range(R)] for k in range(2)]
        abs_sum = [s.sb(f"abs_sum{i}", [P, 2]) for i in range(R)]
        stats = [s.sb(f"stats{i}", [P, 6]) for i in range(R)]
        mv = [s.sb(f"mv{i}", [P, 2]) for i in range(R)]
        rs = [s.sb(f"rs{i}", [P, 2]) for i in range(R)]
        half = s.sb("half", [P, 1])
        turned = [s.bank(f"turned{i}") for i in range(2)]

        consts_in, ready = s.sem("consts_in"), s.sem("ready")
        xz_in = [s.sem(f"xz_in{i}") for i in range(NC)]
        abs_done, keep0_done = s.sem("abs_done"), s.sem("keep0_done")
        y_done, stats_done, mv_done, ve_done = s.sem("y_done"), s.sem("stats_done"), s.sem("mv_done"), s.sem("ve_done")
        rstd_done, centred, xn_done = s.sem("rstd_done"), s.sem("centred"), s.sem("xn_done")
        x1_done = s.sem("x1_done")
        abs1_done, keep1_done = s.sem("abs1_done"), s.sem("keep1_done")
        turn_done, x1t_done = s.sem("turn_done"), s.sem("x1t_done")
        passed = s.sem("passed")
        out = [s.sem(f"out{i}") for i in range(R)]

        block = s.block()

        @block.sync
        def _(sp):
            def load(b, c):
                wait(sp, y_done, NC * (b - 1) + c + 1)
                sp.dma_start(x[c][:, :], x_rows[b, c * P:(c + 1) * P, :]).then_inc(xz_in[c], 16)
                sp.dma_start(z[c][:, :, :], z_groups.rearrange("(b g) s f -> b s g f", g=NG)[b, c * P:(c + 1) * P, :, :])\
                  .then_inc(xz_in[c], 16)

            def store(b, c):
                n, i = NC * b + c, c % R
                wait_apart(sp, x1_done, n + 1, passed)
                sp.dma_start(x1_rows[b, c * P:(c + 1) * P, :], x1[i][:, :]).then_inc(out[i], 16)
                sp.wait_ge(keep1_done, n + 1)
                sp.dma_start(key_mask[b, c * P:(c + 1) * P].unsqueeze(1), keep1[:, NC * b + c, :])\
                  .then_inc(out[i], 16)
                sp.wait_ge(x1t_done, n + 1)
                sp.dma_start(x1t[b, :, c * P:(c + 1) * P].rearrange("(t p) s -> p t s", p=P), x1t_sb[i][:, :, :])\
                  .then_inc(out[i], 16)

            def batch(b):
                for c in range(NC):
                    if tile_after(b, c, AHEAD):
                        load(*tile_after(b, c, AHEAD))
                    if tile_before(b, c, 2):
                        store(*tile_before(b, c, 2))

            sp.dma_start(g_sb[:, :], g_row.partition_broadcast(P)).then_inc(consts_in, 16)
            sp.dma_start(b_sb[:, :], b_row.partition_broadcast(P)).then_inc(consts_in, 16)
            for c in range(AHEAD):
                load(0, c)
            batches(sp, batch)
            store(B - 1, NC - 2)
            store(B - 1, NC - 1)
            for i in range(R):
                sp.wait_ge(out[i], 48 * B * NC // R)

        @block.vector
        def _(dve):
            def mask0(b, c):
                n, i = NC * b + c, c % R
                dve.wait_ge(abs_done, n + 1)
                dve.tensor_scalar(keep0[:, n, :], abs_sum[i][:, 0:1], 0.0, None, ALU.is_gt).then_inc(keep0_done, 1)

            def mask1(b, c):
                n, i = NC * b + c, c % R
                dve.wait_ge(abs1_done, n + 1)
                dve.tensor_scalar(keep1[:, n, :], abs_sum[i][:, 1:2], 0.0, None, ALU.is_gt).then_inc(keep1_done, 1)

            def residual(b, c):
                n, i = NC * b + c, c % R
                dve.wait_ge(xz_in[c], 32 * (b + 1))
                dve.wait_ge(keep0_done, n + 1)
                wait(dve, xn_done, n - R + 1)
                dve.scalar_tensor_tensor(y[i][:, :], z[c][:, :, :].rearrange("p g f -> p (g f)"), keep0[:, n, :],
                                         x[c][:, :], ALU.mult, ALU.add).then_inc(y_done, 1)

            def stats_of(b, c):
                n, i = NC * b + c, c % R
                dve.wait_ge(y_done, n + 1)
                dve.bn_stats(stats[i][:, :], y[i][:, :]).then_inc(stats_done, 1)

            def moments(b, c):
                n, i = NC * b + c, c % R
                wait_apart(dve, stats_done, n + 1, passed)
                dve.bn_aggr(mv[i][:, :], stats[i][:, :]).then_inc(mv_done, 1)
                dve.wait_ge(mv_done, n + 1)
                dve.tensor_scalar(rs[i][:, 0:1], mv[i][:, 1:2], EPS, None, ALU.add).then_inc(ve_done, 1)

            def centre(b, c):
                n, i = NC * b + c, c % R
                dve.wait_ge(mv_done, n + 1)
                dve.scalar_tensor_tensor(y[i][:, :], y[i][:, :], mv[i][:, 0:1], g_sb[:, :], ALU.subtract, ALU.mult)\
                   .then_inc(centred, 1)

            def batch(b):
                for c in range(NC):
                    residual(b, c)
                    if tile_after(b, c, 1):
                        mask0(*tile_after(b, c, 1))
                    if tile_before(b, c, 3):
                        mask1(*tile_before(b, c, 3))
                    stats_of(b, c)
                    if tile_before(b, c, 1):
                        centre(*tile_before(b, c, 1))
                    moments(b, c)

            dve.memset(half[:, :], -0.5).then_inc(ready, 1)
            dve.wait_ge(consts_in, 32)
            mask0(0, 0)
            batches(dve, batch)
            centre(B - 1, NC - 1)
            for c in range(NC - 3, NC):
                mask1(B - 1, c)

        @block.gpsimd
        def _(pool):
            def rstd(b, c):
                n, i = NC * b + c, c % R
                pool.wait_ge(ve_done, n + 1)
                pool.tensor_tensor(rs[i][:, 1:2], rs[i][:, 0:1], half[:, :], ALU.pow).then_inc(rstd_done, 1)

            def add_shift(b, c):
                n, i = NC * b + c, c % R
                pool.wait_ge(xn_done, n + 1)
                if c >= R:
                    pool.wait_ge(out[i], 48 * (2 * b + 1))
                else:
                    wait(pool, out[i], 48 * 2 * b)
                pool.tensor_tensor(x1[i][:, :], xn[i][:, :], b_sb[:, :], ALU.add).then_inc(x1_done, 1)

            def batch(b):
                for c in range(NC):
                    rstd(b, c)
                    if tile_before(b, c, 1):
                        add_shift(*tile_before(b, c, 1))

            pool.wait_ge(ready, 1)
            pool.wait_ge(consts_in, 32)
            batches(pool, batch)
            add_shift(B - 1, NC - 1)

        @block.scalar
        def _(act):
            def abs_x(b, c):
                n, i = NC * b + c, c % R
                act.wait_ge(xz_in[c], 32 * (b + 1))
                wait(act, keep0_done, n - R + 1)
                act.activation(abs_out[0][i][:, :], x[c][:, :], ACT.Abs, accum_out=abs_sum[i][:, 0:1]).then_inc(abs_done, 1)

            def abs_x1(b, c):
                n, i = NC * b + c, c % R
                act.wait_ge(x1_done, n + 1)
                wait(act, keep1_done, n - R + 1)
                act.activation(abs_out[1][i][:, :], x1[i][:, :], ACT.Abs, accum_out=abs_sum[i][:, 1:2]).then_inc(abs1_done, 1)

            def normalize(b, c):
                n, i = NC * b + c, c % R
                act.wait_ge(centred, n + 1)
                act.wait_ge(rstd_done, n + 1)
                wait(act, x1_done, n - R + 1)
                act.activation(xn[i][:, :], y[i][:, :], ACT.Copy, scale=rs[i][:, 1:2])\
                   .then_inc(xn_done, 1)

            def copy_turned(b, c):
                n, i = NC * b + c, c % R
                act.wait_ge(turn_done, n + 1)
                if c >= R:
                    act.wait_ge(out[i], 48 * (2 * b + 1))
                else:
                    wait(act, out[i], 48 * 2 * b)
                act.activation(x1t_sb[i][:, :, :], turned[c % 2][:, :].rearrange("p (t s) -> p t s", t=ND), ACT.Copy)\
                   .then_inc(x1t_done, 1)

            def batch(b):
                for c in range(NC):
                    if tile_after(b, c, 2):
                        abs_x(*tile_after(b, c, 2))
                    if tile_before(b, c, 2):
                        abs_x1(*tile_before(b, c, 2))
                    if tile_before(b, c, 1):
                        normalize(*tile_before(b, c, 1))
                    if tile_before(b, c, 2):
                        copy_turned(*tile_before(b, c, 2))

            abs_x(0, 0)
            abs_x(0, 1)
            batches(act, batch)
            abs_x1(B - 1, NC - 2)
            normalize(B - 1, NC - 1)
            abs_x1(B - 1, NC - 1)
            copy_turned(B - 1, NC - 2)
            copy_turned(B - 1, NC - 1)

        @block.tensor
        def _(pe):
            def batch(b):
                for c in range(NC):
                    n = NC * b + c
                    pe.wait_ge(x1_done, n + 1)
                    wait(pe, x1t_done, n - 1)
                    for d in range(ND):
                        last = pe.transpose(turned[c % 2][:, d * P:(d + 1) * P], x1[c % R][:, d * P:(d + 1) * P],
                                            ident[:, :])
                    last.then_inc(turn_done, 1)

            batches(pe, batch)


def mlp(nc, stage, ident, x1_rows, z_groups, keep0, keep1, gains, w1, b1, w2, b2, x3_rows):
    with ExitStack() as ctx:
        s = Space(nc, ctx, stage)
        R = 4
        gain = [s.sb(f"gain{i}", [P, D]) for i in range(2)]
        shift = [s.sb(f"shift{i}", [P, D]) for i in range(2)]
        w_raw = s.sb("w_raw", [P, ND, D])
        w_hi = [s.sb(f"w_hi{i}", [P, ND, D], F32R) for i in range(2)]
        w_lo = [s.sb(f"w_lo{i}", [P, ND, D], F32R) for i in range(2)]
        b1_sb = s.sb("b1", [P, ND])
        b2_sb = s.sb("b2", [P, D])
        b2_part = [s.sb(f"b2{t}", [P, D], F32R) for t in ("hi", "lo")]
        ident_r = s.sb("ident_r", [P, P], F32R)
        half = s.sb("half", [P, 1])
        x1 = [s.sb(f"x1{i}", [P, D]) for i in range(R)]
        z = [s.sb(f"z{i}", [P, HPG, P]) for i in range(R)]
        x2 = [s.sb(f"x2{i}", [P, D]) for i in range(NC)]
        y = [[s.sb(f"y{k}{i}", [P, D]) for i in range(R)] for k in range(2)]
        x3 = [s.sb(f"x3{i}", [P, D]) for i in range(R)]
        stats = [[s.sb(f"stats{k}{i}", [P, 6]) for i in range(R)] for k in range(2)]
        mv = [[s.sb(f"mv{k}{i}", [P, 2]) for i in range(R)] for k in range(2)]
        rs = [[s.sb(f"rs{k}{i}", [P, 2]) for i in range(R)] for k in range(2)]
        x2t = [s.sb(f"x2t{t}", [P, ND, HALF], F32R) for t in ("hi", "lo")]
        hid = [s.sb(f"hid{i}", [P, HALF]) for i in range(ND)]
        hid_part = [s.sb(f"hid{t}", [P, ND, HALF], F32R) for t in ("hi", "lo")]
        turned = [s.bank(f"turned{i}") for i in range(2)]
        up = [s.bank(f"up{i}") for i in range(2)]
        down = [s.bank(f"down{i}") for i in range(2)]

        consts_in, w_in, w_split_hi, w_split = (s.sem(n) for n in ("consts_in", "w_in", "w_split_hi", "w_split"))
        norm_in = [s.sem(f"norm_in{k}") for k in range(2)]
        ready = s.sem("ready")
        b2_hi, b2_split = s.sem("b2_hi"), s.sem("b2_split")
        xz_in = [s.sem(f"xz_in{i}") for i in range(R)]
        y_done, stats_done, mv_done, ve_done, rstd_done, centred, xn_done, norm_done = (
            [s.sem(f"{n}{k}") for k in range(2)] for n in
            ("y_done", "stats_done", "mv_done", "ve_done", "rstd_done", "centred", "xn_done", "norm_done"))
        turn_done, x2t_hi, x2t_lo = s.sem("turn_done"), s.sem("x2t_hi"), s.sem("x2t_lo")
        up_done, hid_done, hid_lo = s.sem("up_done"), s.sem("hid_done"), s.sem("hid_lo")
        down_done = s.sem("down_done")
        passed = s.sem("passed")
        out = [s.sem(f"out{i}") for i in range(R)]

        def unit_after(b, h):
            if h == 0:
                return b, 1
            return None if isinstance(b, int) and b == B - 1 else (b + 1, 0)

        def unit_before(b, h):
            if h == 1:
                return b, 0
            return None if isinstance(b, int) and b == 0 else (b - 1, 1)

        def number(b, h, t):
            return NC * b + R * h + t

        block = s.block()

        @block.sync
        def _(sp):
            def load(b, h, t):
                c = R * h + t
                wait(sp, y_done[0], number(b, h, t) - R + 1)
                sp.dma_start(x1[t][:, :], x1_rows[b, c * P:(c + 1) * P, :]).then_inc(xz_in[t], 16)
                sp.dma_start(z[t][:, :, :], z_groups.rearrange("(b g) s f -> b s g f", g=NG)[b, c * P:(c + 1) * P, :, :])\
                  .then_inc(xz_in[t], 16)

            def store(b, h, t):
                c = R * h + t
                sp.wait_ge(norm_done[1], number(b, h, t) + 1)
                sp.dma_start(x3_rows[b, c * P:(c + 1) * P, :], x3[t][:, :]).then_inc(out[t], 16)

            def batch(b):
                for h in range(2):
                    nxt = unit_after(b, h)
                    for t in range(R):
                        if nxt and unit_after(*nxt):
                            load(*unit_after(*nxt), t)
                    if unit_before(b, h):
                        store(*unit_before(b, h), R - 1)
                    for t in range(R - 1):
                        store(b, h, t)

            def load_norm(k):
                for tile, row in ((gain[k], gains[2 * k]), (shift[k], gains[2 * k + 1])):
                    sp.dma_start(tile[:, :], row.partition_broadcast(P)).then_inc(norm_in[k], 16)

            load(0, 0, 0)
            load_norm(0)
            for t in range(1, R):
                load(0, 0, t)
            sp.dma_start(w_raw[:, :, :], w1.rearrange("(t p) n -> p t n", p=P)).then_inc(w_in, 16)
            load_norm(1)
            sp.dma_start(b1_sb[:, :], b1).then_inc(consts_in, 16)
            sp.dma_start(b2_sb[:, :], b2.partition_broadcast(P)).then_inc(consts_in, 16)
            sp.wait_ge(w_split, 1)
            sp.dma_start(w_raw[:, :, :], w2.rearrange("(t p) n -> p t n", p=P)).then_inc(w_in, 16)
            for t in range(R):
                load(0, 1, t)
            batches(sp, batch)
            store(B - 1, 1, R - 1)
            for i in range(R):
                sp.wait_ge(out[i], 16 * 2 * B)

        @block.vector
        def _(dve):
            def moments(k, b, h, t):
                n = number(b, h, t)
                dve.wait_ge(y_done[k], n + 1)
                dve.bn_stats(stats[k][t][:, :], y[k][t][:, :]).then_inc(stats_done[k], 1)
                wait_apart(dve, stats_done[k], n + 1, passed)
                dve.bn_aggr(mv[k][t][:, :], stats[k][t][:, :]).then_inc(mv_done[k], 1)
                dve.wait_ge(mv_done[k], n + 1)
                dve.tensor_scalar(rs[k][t][:, 0:1], mv[k][t][:, 1:2], EPS, None, ALU.add).then_inc(ve_done[k], 1)
                dve.scalar_tensor_tensor(y[k][t][:, :], y[k][t][:, :], mv[k][t][:, 0:1], gain[k][:, :],
                                         ALU.subtract, ALU.mult).then_inc(centred[k], 1)

            def residual2(b, h, t):
                n = number(b, h, t)
                dve.wait_ge(xz_in[t], 32 * (2 * b + h + 1))
                wait(dve, norm_done[0], n - R + 1)
                dve.scalar_tensor_tensor(y[0][t][:, :], z[t][:, :, :].rearrange("p g f -> p (g f)"), keep1[:, n, :],
                                         x1[t][:, :], ALU.mult, ALU.add).then_inc(y_done[0], 1)
                moments(0, b, h, t)

            def residual3(b, h, t):
                n = number(b, h, t)
                dve.wait_ge(down_done, n + 1)
                wait(dve, norm_done[1], n - R + 1)
                dve.scalar_tensor_tensor(y[1][t][:, :], down[t % 2][:, :], keep0[:, n, :], x2[R * h + t][:, :],
                                         ALU.mult, ALU.add).then_inc(y_done[1], 1)
                moments(1, b, h, t)

            def turned_lo(b, h, t):
                n = number(b, h, t)
                cols = slice(t * P, (t + 1) * P)
                dve.wait_ge(x2t_hi, n + 1)
                dve.tensor_tensor(x2t[1][:, :, cols], turned[t % 2][:, :].rearrange("p (d s) -> p d s", d=ND),
                                  f32(x2t[0][:, :, cols]), ALU.subtract).then_inc(x2t_lo, 1)

            def hidden_lo(b, h, f):
                n = number(b, h, f)
                dve.wait_ge(hid_done, 2 * (n + 1))
                dve.tensor_tensor(hid_part[1][:, f, :], hid[f][:, :], f32(hid_part[0][:, f, :]), ALU.subtract)\
                   .then_inc(hid_lo, 1)

            def batch(b):
                for h in range(2):
                    nxt = unit_after(b, h)
                    for f in range(ND):
                        hidden_lo(b, h, f)
                        if nxt:
                            residual2(*nxt, f)
                    for t in range(R):
                        if nxt:
                            turned_lo(*nxt, t)
                        residual3(b, h, t)

            dve.memset(half[:, :], -0.5).then_inc(ready, 1)
            dve.tensor_copy(ident_r[:, :], ident[:, :]).then_inc(ready, 1)
            def split_w(i):
                dve.wait_ge(w_in, 16 * (i + 1))
                dve.tensor_copy(w_hi[i][:, :, :], w_raw[:, :, :]).then_inc(w_split_hi, 1)
                dve.wait_ge(w_split_hi, i + 1)
                dve.tensor_tensor(w_lo[i][:, :, :], w_raw[:, :, :], f32(w_hi[i][:, :, :]), ALU.subtract)\
                   .then_inc(w_split, 1)

            dve.wait_ge(norm_in[0], 32)
            for t in range(R):
                residual2(0, 0, t)
            split_w(0)
            for t in range(R):
                turned_lo(0, 0, t)
            dve.wait_ge(norm_in[1], 32)
            dve.wait_ge(consts_in, 32)
            split_w(1)
            dve.tensor_copy(b2_part[0][:, :], b2_sb[:, :]).then_inc(b2_hi, 1)
            dve.wait_ge(b2_hi, 1)
            dve.tensor_tensor(b2_part[1][:, :], b2_sb[:, :], f32(b2_part[0][:, :]), ALU.subtract).then_inc(b2_split, 1)
            batches(dve, batch)

        @block.gpsimd
        def _(pool):
            def rstd(k, b, h, t):
                pool.wait_ge(ve_done[k], number(b, h, t) + 1)
                pool.tensor_tensor(rs[k][t][:, 1:2], rs[k][t][:, 0:1], half[:, :], ALU.pow).then_inc(rstd_done[k], 1)

            def add_shift(k, b, h, t):
                n = number(b, h, t)
                pool.wait_ge(xn_done[k], n + 1)
                if k == 0:
                    wait(pool, y_done[1], n - 2 * R + 1)
                else:
                    wait(pool, out[t], 16 * (2 * b + h))
                dst = x2[R * h + t] if k == 0 else x3[t]
                pool.tensor_tensor(dst[:, :], y[k][t][:, :], shift[k][:, :], ALU.add).then_inc(norm_done[k], 1)

            def batch(b):
                for h in range(2):
                    nxt = unit_after(b, h)
                    if unit_before(b, h):
                        add_shift(1, *unit_before(b, h), R - 1)
                    for t in range(R):
                        if nxt:
                            rstd(0, *nxt, t)
                            if t:
                                add_shift(0, *nxt, t - 1)
                    if nxt:
                        add_shift(0, *nxt, R - 1)
                    for t in range(R):
                        rstd(1, b, h, t)
                        if t:
                            add_shift(1, b, h, t - 1)

            pool.wait_ge(ready, 2)
            for k in range(2):
                pool.wait_ge(norm_in[k], 32)
            for t in range(R):
                rstd(0, 0, 0, t)
                if t:
                    add_shift(0, 0, 0, t - 1)
            add_shift(0, 0, 0, R - 1)
            batches(pool, batch)
            add_shift(1, B - 1, 1, R - 1)

        @block.scalar
        def _(act):
            def normalize(k, b, h, t):
                act.wait_ge(centred[k], number(b, h, t) + 1)
                act.wait_ge(rstd_done[k], number(b, h, t) + 1)
                act.activation(y[k][t][:, :], y[k][t][:, :], ACT.Copy, scale=rs[k][t][:, 1:2])\
                   .then_inc(xn_done[k], 1)

            def turned_hi(b, h, t):
                n = number(b, h, t)
                act.wait_ge(turn_done, n + 1)
                wait(act, up_done, NC * b + R * h)
                act.activation(x2t[0][:, :, t * P:(t + 1) * P], turned[t % 2][:, :].rearrange("p (d s) -> p d s", d=ND),
                               ACT.Copy).then_inc(x2t_hi, 1)

            def hidden(b, h, f):
                n = number(b, h, f)
                act.wait_ge(up_done, n + 1)
                wait(act, hid_lo, n - ND + 1)
                wait(act, down_done, R * 2 * b + R * h)
                for dst in (hid[f][:, :], hid_part[0][:, f, :]):
                    act.activation(dst, up[f % 2][:, :], ACT.Relu, bias=b1_sb[:, f:f + 1]).then_inc(hid_done, 1)

            def batch(b):
                for h in range(2):
                    nxt = unit_after(b, h)
                    if unit_before(b, h):
                        normalize(1, *unit_before(b, h), R - 1)
                    for f in range(ND):
                        hidden(b, h, f)
                        if nxt and f:
                            normalize(0, *nxt, f - 1)
                    if nxt:
                        normalize(0, *nxt, R - 1)
                    for t in range(R):
                        if nxt:
                            turned_hi(*nxt, t)
                        if t:
                            normalize(1, b, h, t - 1)

            for t in range(R):
                normalize(0, 0, 0, t)
            for t in range(R):
                turned_hi(0, 0, t)
            act.wait_ge(consts_in, 32)
            batches(act, batch)
            normalize(1, B - 1, 1, R - 1)

        @block.tensor
        def _(pe):
            def turn(b, h, t):
                n = number(b, h, t)
                pe.wait_ge(norm_done[0], n + 1)
                wait(pe, x2t_lo, n - 1)
                for d in range(ND):
                    last = pe.transpose(turned[t % 2][:, d * P:(d + 1) * P], x2[R * h + t][:, d * P:(d + 1) * P], ident[:, :])
                last.then_inc(turn_done, 1)

            def up_block(b, h, f):
                n = number(b, h, f)
                if f == 0:
                    pe.wait_ge(w_split, 1)
                    pe.wait_ge(x2t_lo, number(b, h, R))
                wait(pe, hid_done, 2 * (n - 1))
                for i, (wt, xt) in enumerate(TERMS):
                    for d in range(ND):
                        last = pe.matmul(up[f % 2][:, :], (w_hi, w_lo)[wt][0][:, d, f * P:(f + 1) * P], x2t[xt][:, d, :],
                                         start=(i == 0 and d == 0), stop=(i == 2 and d == ND - 1))
                last.then_inc(up_done, 1)

            def down_tile(b, h, t):
                n = number(b, h, t)
                if t == 0:
                    pe.wait_ge(w_split, 2)
                    pe.wait_ge(b2_split, 1)
                    pe.wait_ge(hid_lo, number(b, h, ND))
                wait(pe, y_done[1], n - 1)
                for i, (xt, wt) in enumerate(TERMS):
                    for f in range(ND):
                        pe.matmul(down[t % 2][:, :], hid_part[xt][:, f, t * P:(t + 1) * P], (w_hi, w_lo)[wt][1][:, f, :],
                                  start=(i == 0 and f == 0), stop=False)
                for part in range(2):
                    last = pe.matmul(down[t % 2][:, :], ident_r[:, :], b2_part[part][:, :], start=False, stop=(part == 1))
                last.then_inc(down_done, 1)

            def batch(b):
                for h in range(2):
                    nxt = unit_after(b, h)
                    for f in range(ND):
                        up_block(b, h, f)
                    for t in range(R):
                        if nxt and t == 0:
                            turn(*nxt, 0)
                        if nxt and t + 1 < R:
                            turn(*nxt, t + 1)
                        down_tile(b, h, t)

            for t in range(R):
                turn(0, 0, t)
            batches(pe, batch)


def attend_context(nc, stage, ident, x3_rows, ctx_rows, ctxt, out_rows):
    with ExitStack() as stack:
        s = Space(nc, stack, stage)
        R = 4
        raw_t = [s.sb(f"raw_t{h}", [P, ND, HALF]) for h in range(NS)]
        raw = [s.sb(f"raw{h}", [P, NC // 2, D]) for h in range(2)]
        kt = [s.sb(f"kt{t}", [P, ND, S], F32R) for t in ("hi", "lo")]
        kv = [s.sb(f"kv{t}", [P, NC, D], F32R) for t in ("hi", "lo")]
        x3 = [s.sb(f"x3{i}", [P, D]) for i in range(R)]
        x3t = [[s.sb(f"x3t{i}{t}", [P, ND, P], F32R) for t in ("hi", "lo")] for i in range(2)]
        mparts = [s.sb(f"mparts{i}", [P, NS]) for i in range(2)]
        negmax = [s.sb(f"negmax{i}", [P, 1]) for i in range(2)]
        w = [s.sb(f"w{i}", [P, S]) for i in range(2)]
        sums = [s.sb(f"sums{i}", [P, NS]) for i in range(2)]
        total = [s.sb(f"total{i}", [P, 2]) for i in range(2)]
        wt = [s.sb(f"wt{t}", [P, NC, P], F32R) for t in ("hi", "lo")]
        o = [s.sb(f"o{i}", [P, D]) for i in range(2)]
        turned = s.bank("turned")
        e = [s.bank(f"e{h}") for h in range(NS)]
        turned_w = [s.bank(f"turned_w{h}") for h in range(NS)]
        acc = [s.bank(f"acc{i}") for i in range(2)]

        raw_t_in = [s.sem(f"raw_t_in{h}") for h in range(NS)]
        raw_in = [s.sem(f"raw_in{h}") for h in range(2)]
        kt_hi, kt_split, kv_hi, kv_split = (s.sem(n) for n in ("kt_hi", "kt_split", "kv_hi", "kv_split"))
        x3_in = [s.sem(f"x3_in{i}") for i in range(R)]
        x3_turned, x3t_hi, x3t_lo = (s.sem(n) for n in ("x3_turned", "x3t_hi", "x3t_lo"))
        e_done, mpart_done, negmax_done, exp_done = (s.sem(n) for n in ("e_done", "mpart_done", "negmax_done", "exp_done"))
        w_turned, wt_hi, wt_lo = (s.sem(n) for n in ("w_turned", "wt_hi", "wt_lo"))
        acc_done, sum_done, recip_done, o_done = (s.sem(n) for n in ("acc_done", "sum_done", "recip_done", "o_done"))
        out = [s.sem(f"out{i}") for i in range(2)]
        passed = s.sem("passed")

        block = s.block()

        @block.sync
        def _(sp):
            def load_context(b):
                for h in range(NS):
                    wait(sp, kt_split, 2 * (b - 1) + h + 1)
                    sp.dma_start(raw_t[h][:, :, :], ctxt[b, :, h * HALF:(h + 1) * HALF].rearrange("(t p) s -> p t s", p=P))\
                      .then_inc(raw_t_in[h], 16)
                for h in range(2):
                    wait(sp, kv_split, 2 * (b - 1) + h + 1)
                    sp.dma_start(raw[h][:, :, :], ctx_rows[b, h * HALF:(h + 1) * HALF, :].rearrange("(c p) d -> p c d", p=P))\
                      .then_inc(raw_in[h], 16)

            def load(b, c):
                n = NC * b + c
                wait(sp, o_done, n - R + 1)
                sp.dma_start(x3[c % R][:, :], x3_rows[b, c * P:(c + 1) * P, :]).then_inc(x3_in[c % R], 16)

            def store(b, c):
                wait_apart(sp, o_done, NC * b + c + 1, passed)
                sp.dma_start(out_rows[b, c * P:(c + 1) * P, :], o[c % 2][:, :]).then_inc(out[c % 2], 16)

            def batch(b):
                for c in range(NC):
                    if tile_before(b, c, 1):
                        store(*tile_before(b, c, 1))
                    if tile_after(b, c, 3):
                        load(*tile_after(b, c, 3))
                    if c == 1 and tile_after(b, c, NC):
                        load_context(b + 1)

            load(0, 0)
            load_context(0)
            load(0, 1)
            load(0, 2)
            batches(sp, batch)
            store(B - 1, NC - 1)
            for i in range(2):
                sp.wait_ge(out[i], 16 * B * NC // 2)

        @block.tensor
        def _(pe):
            def turn_x3(b, c):
                n = NC * b + c
                pe.wait_ge(x3_in[c % R], 16 * (2 * b + c // R + 1))
                wait(pe, x3t_lo, n)
                for d in range(ND):
                    last = pe.transpose(turned[:, d * P:(d + 1) * P], x3[c % R][:, d * P:(d + 1) * P], ident[:, :])
                last.then_inc(x3_turned, 1)

            def scores(b, c):
                n = NC * b + c
                pe.wait_ge(x3t_lo, n + 1)
                for h in range(NS):
                    if c == 0:
                        pe.wait_ge(kt_split, 2 * b + h + 1)
                    wait(pe, exp_done, NS * (n - 1) + h + 1)
                    for i, (xt, k) in enumerate(TERMS):
                        for d in range(ND):
                            last = pe.matmul(e[h][:, :], x3t[c % 2][xt][:, d, :], kt[k][:, d, h * HALF:(h + 1) * HALF],
                                             start=(i == 0 and d == 0), stop=(i == 2 and d == ND - 1))
                    last.then_inc(e_done, 1)

            def turn_weights(b, c):
                n = NC * b + c
                for h in range(NS):
                    pe.wait_ge(exp_done, NS * n + h + 1)
                    wait(pe, wt_lo, NS * (n - 1) + h + 1)
                    for j in range(4):
                        last = pe.transpose(turned_w[h][:, j * P:(j + 1) * P],
                                            w[c % 2][:, (4 * h + j) * P:(4 * h + j + 1) * P], ident[:, :])
                    last.then_inc(w_turned, 1)

            def weighted(b, c):
                n = NC * b + c
                wait(pe, o_done, n - 1)
                for h in range(NS):
                    pe.wait_ge(wt_lo, NS * n + h + 1)
                    if c == 0:
                        pe.wait_ge(kv_split, 2 * b + h + 1)
                    for i, (p, k) in enumerate(TERMS):
                        for j in range(4):
                            last = pe.matmul(acc[c % 2][:, :], wt[p][:, 4 * h + j, :], kv[k][:, 4 * h + j, :],
                                             start=(h == 0 and i == 0 and j == 0),
                                             stop=(h == NS - 1 and i == 2 and j == 3))
                last.then_inc(acc_done, 1)

            def batch(b):
                for c in range(NC):
                    turn_weights(b, c)
                    if tile_after(b, c, 1):
                        scores(*tile_after(b, c, 1))
                    if tile_after(b, c, 2):
                        turn_x3(*tile_after(b, c, 2))
                    weighted(b, c)

            turn_x3(0, 0)
            scores(0, 0)
            turn_x3(0, 1)
            batches(pe, batch)

        @block.scalar
        def _(act):
            def x3_hi(b, c):
                n = NC * b + c
                act.wait_ge(x3_turned, n + 1)
                wait(act, e_done, NS * (n - 1))
                act.activation(x3t[c % 2][0][:, :, :], turned[:, :].rearrange("p (d s) -> p d s", d=ND), ACT.Copy)\
                   .then_inc(x3t_hi, 1)

            def exps(b, c):
                n = NC * b + c
                act.wait_ge(negmax_done, n + 1)
                wait(act, w_turned, NS * (n - 1))
                wait(act, sum_done, n - 1)
                for h in range(NS):
                    act.activation(w[c % 2][:, h * HALF:(h + 1) * HALF], e[h][:, :], ACT.Exp, bias=negmax[c % 2][:, :],
                                   accum_out=sums[c % 2][:, h:h + 1]).then_inc(exp_done, 1)

            def weights_hi(b, c):
                n = NC * b + c
                wait(act, acc_done, n)
                for h in range(NS):
                    act.wait_ge(w_turned, NS * n + h + 1)
                    act.activation(wt[0][:, 4 * h:4 * h + 4, :], turned_w[h][:, :].rearrange("p (j s) -> p j s", j=4),
                                   ACT.Copy).then_inc(wt_hi, 1)

            def batch(b):
                for c in range(NC):
                    weights_hi(b, c)
                    if tile_after(b, c, 2):
                        x3_hi(*tile_after(b, c, 2))
                    if tile_after(b, c, 1):
                        exps(*tile_after(b, c, 1))

            x3_hi(0, 0)
            x3_hi(0, 1)
            exps(0, 0)
            batches(act, batch)

        @block.vector
        def _(dve):
            def x3_lo(b, c):
                n = NC * b + c
                dve.wait_ge(x3t_hi, n + 1)
                dve.tensor_tensor(x3t[c % 2][1][:, :, :], turned[:, :].rearrange("p (d s) -> p d s", d=ND),
                                  f32(x3t[c % 2][0][:, :, :]), ALU.subtract).then_inc(x3t_lo, 1)

            def maxima(b, c):
                n = NC * b + c
                wait(dve, negmax_done, n - 1)
                for h in range(NS):
                    dve.wait_ge(e_done, NS * n + h + 1)
                    dve.tensor_reduce(mparts[c % 2][:, h:h + 1], e[h][:, :], AX.X, ALU.max).then_inc(mpart_done, 1)
                dve.wait_ge(mpart_done, NS * (n + 1))
                wait(dve, exp_done, NS * (n - 1))
                dve.tensor_reduce(negmax[c % 2][:, :], mparts[c % 2][:, :], AX.X, ALU.max, negate=True)\
                   .then_inc(negmax_done, 1)

            def weights_lo(b, c):
                n = NC * b + c
                for h in range(NS):
                    dve.wait_ge(wt_hi, NS * n + h + 1)
                    dve.tensor_tensor(wt[1][:, 4 * h:4 * h + 4, :], turned_w[h][:, :].rearrange("p (j s) -> p j s", j=4),
                                      f32(wt[0][:, 4 * h:4 * h + 4, :]), ALU.subtract).then_inc(wt_lo, 1)

            def outputs(b, c):
                n = NC * b + c
                dve.wait_ge(exp_done, NS * (n + 1))
                wait(dve, o_done, n - 1)
                dve.tensor_tensor(total[c % 2][:, 0:1], sums[c % 2][:, 0:1], sums[c % 2][:, 1:2], ALU.add)\
                   .then_inc(sum_done, 1)
                dve.wait_ge(sum_done, n + 1)
                dve.reciprocal(total[c % 2][:, 1:2], total[c % 2][:, 0:1]).then_inc(recip_done, 1)
                dve.wait_ge(recip_done, n + 1)
                dve.wait_ge(acc_done, n + 1)
                if c >= 2:
                    dve.wait_ge(out[c % 2], 16 * (4 * b + c // 2))
                else:
                    wait(dve, out[c % 2], 16 * 4 * b)
                dve.scalar_tensor_tensor(o[c % 2][:, :], acc[c % 2][:, :], total[c % 2][:, 1:2], x3[c % R][:, :],
                                         ALU.mult, ALU.add).then_inc(o_done, 1)

            def split_kt(b):
                wait(dve, e_done, NS * NC * b)
                for h in range(NS):
                    cols = slice(h * HALF, (h + 1) * HALF)
                    dve.wait_ge(raw_t_in[h], 16 * (b + 1))
                    dve.tensor_copy(kt[0][:, :, cols], raw_t[h][:, :, :]).then_inc(kt_hi, 1)
                    dve.wait_ge(kt_hi, 2 * b + h + 1)
                    dve.tensor_tensor(kt[1][:, :, cols], raw_t[h][:, :, :], f32(kt[0][:, :, cols]), ALU.subtract)\
                       .then_inc(kt_split, 1)

            def split_kv(b):
                wait(dve, acc_done, NC * b)
                for h in range(2):
                    tiles = slice(h * 4, h * 4 + 4)
                    dve.wait_ge(raw_in[h], 16 * (b + 1))
                    dve.tensor_copy(kv[0][:, tiles, :], raw[h][:, :, :]).then_inc(kv_hi, 1)
                    dve.wait_ge(kv_hi, 2 * b + h + 1)
                    dve.tensor_tensor(kv[1][:, tiles, :], raw[h][:, :, :], f32(kv[0][:, tiles, :]), ALU.subtract)\
                       .then_inc(kv_split, 1)

            def batch(b):
                for c in range(NC):
                    weights_lo(b, c)
                    if tile_after(b, c, 2):
                        x3_lo(*tile_after(b, c, 2))
                    if tile_after(b, c, 1):
                        maxima(*tile_after(b, c, 1))
                    outputs(b, c)
                    if c == NC - 2 and tile_after(b, c, NC):
                        split_kt(b + 1)
                    if c == NC - 1 and tile_after(b, c, NC):
                        split_kv(b + 1)

            x3_lo(0, 0)
            split_kt(0)
            x3_lo(0, 1)
            maxima(0, 0)
            split_kv(0)
            batches(dve, batch)


def build(nc, x, xt, ctx_rows, ctxt, wq1, wk1, wv1, wq2, wk2, wv2, g1, s1, g2, s2, g3, s3, w1, b1, w2, b2,
          ident, blk17, tri, sel, iota, out):
    def scratch(name, shape):
        return nc.dram_tensor(name, shape, F32, kind="Internal").ap()

    scr = (scratch("q_split", [2, B * D, S]), scratch("k_split", [2, B * D, S]),
           scratch("v_heads", [B * H, P, NC * DK]), scratch("len_mask", [B * H, S]))
    z_groups = scratch("z_groups", [GROUPS, S, P])
    x1_rows, x1t = scratch("x1_rows", [B, S, D]), scratch("x1t", [B, D, S])
    key_mask = scratch("key_mask", [B, S])
    x3_rows = scratch("x3_rows", [B, S, D])

    with ExitStack() as ctx:
        s = Space(nc, ctx, "all")
        ident_sb = s.sb("ident", [P, P])
        keep0, keep1 = s.sb("keep0", [P, B * NC, 1]), s.sb("keep1", [P, B * NC, 1])
        ident_in = s.sem("ident_in")
        with nc.Block() as block:
            @block.sync
            def _(sp):
                sp.dma_start(ident_sb[:, :], ident).then_inc(ident_in, 16)
                sp.wait_ge(ident_in, 16)

        project(nc, "proj1", xt, xt, None, wq1, wk1, wv1, sel, iota, scr)
        attend(nc, "self", True, ident_sb, blk17, tri, scr, z_groups)
        norm1(nc, "norm1", ident_sb, x, z_groups, g1, s1, keep0, keep1, x1_rows, x1t, key_mask)
        project(nc, "proj2", x1t, ctxt, key_mask, wq2, wk2, wv2, sel, iota, scr)
        attend(nc, "cross", False, ident_sb, blk17, tri, scr, z_groups)
        mlp(nc, "mlp", ident_sb, x1_rows, z_groups, keep0, keep1, (g2, s2, g3, s3), w1, b1, w2, b2, x3_rows)
        attend_context(nc, "last", ident_sb, x3_rows, ctx_rows, ctxt, out)


def layout(inputs):
    L = {k.removeprefix("L0_xattn_"): np.asarray(v) for k, v in inputs.items()}

    def heads(w):
        return w.transpose(1, 0, 2).reshape(D, D)

    ident = np.eye(P, dtype=np.float32)
    blk17 = np.zeros((M_ROWS, NC, P), np.float32)
    blk17[0] = 1
    for j in range(NC):
        blk17[1 + j, j] = blk17[1 + NC + j, j] = 1
    tri = np.zeros((P, HALF), np.float32)
    tri[:, HALF - P:][np.arange(P)[None, :] > np.arange(P)[:, None]] = NEG
    sel = np.zeros((P, NG, H), np.float32)
    for g in range(NG):
        for p in range(P):
            sel[p, g, HPG * g + p // DK] = 1
    iota = np.tile(np.arange(S, dtype=np.float32), (H, 1))
    named = {
        "x": L["x"], "xt": L["x"].transpose(0, 2, 1), "ctx": L["ctx_1024"], "ctxt": L["ctx_1024"].transpose(0, 2, 1),
        "wq1": heads(L["Wq1"]), "wk1": heads(L["Wk1"]), "wv1": heads(L["Wv1"]),
        "wq2": heads(L["Wq2"]), "wk2": heads(L["Wk2"]), "wv2": heads(L["Wv2"]),
        "g1": L["ln1_g"], "s1": L["ln1_b"], "g2": L["ln2_g"], "s2": L["ln2_b"], "g3": L["ln3_g"], "s3": L["ln3_b"],
        "w1": L["fc1_w"].T, "b1": L["fc1_b"].reshape(ND, P).T, "w2": L["fc2_w"].T, "b2": L["fc2_b"],
        "ident": ident, "blk17": blk17, "tri": tri, "sel": sel, "iota": iota,
    }
    return {k: np.ascontiguousarray(v) for k, v in named.items()}


def kernel(**inputs):
    import concourse.bacc as bacc
    from concourse.bass_utils import run_bass_kernel_spmd

    nc = bacc.Bacc("TRN2", target_bir_lowering=False, num_devices=1)
    arrays, args = {}, []
    for name, a in layout(inputs).items():
        arrays[f"in_{name}"] = a
        args.append(nc.dram_tensor(f"in_{name}", a.shape, mybir.dt.from_np(a.dtype), kind="ExternalInput").ap())
    out = nc.dram_tensor("out_rows", [B, S, D], F32, kind="ExternalOutput").ap()
    build(nc, *args, out)
    r = run_bass_kernel_spmd(nc, [arrays], core_ids=[0])
    return r.results[0]["out_rows"]
```
